# Optimizing a Trainium2 kernel written in Bass

```python
import numpy as np
import jax
import jax.numpy as jnp

def _softmax(x, axis=-1):
    return jax.nn.softmax(x, axis=axis)

def _gelu(x):
    return jax.nn.gelu(x, approximate=True)

def _silu(x):
    return jax.nn.silu(x)

def _sigmoid(x):
    return jax.nn.sigmoid(x)

def _layernorm(x, axis=-1, eps=1e-05):
    m = jnp.mean(x, axis=axis, keepdims=True)
    v = jnp.var(x, axis=axis, keepdims=True)
    return (x - m) / jnp.sqrt(v + eps)

def _scatter_add(tgt, idx, src, axis=0):
    return tgt.at[idx].add(src)

def _segment_sum(src, seg, n):
    return jax.ops.segment_sum(src, seg, n)
kernel_name = 'mk_lm_tower_d1_tok_ids1024_r4_3caafe'

def setup_inputs(seed: int=0):
    np.random.seed(seed)
    _w = jnp.asarray

    def _rec_inputs():
        import jax
        import jax.numpy as jnp
        _rk = jax.random.key(seed)
        x = jax.random.randint(jax.random.fold_in(_rk, 1), (128, 128), 0, 12564, jnp.int32)
        return x
    x = _rec_inputs()

    def _L0_tok_setup():
        import jax, jax.numpy as jnp
        import numpy as np
        VOCAB = 50257
        D_MODEL = 256
        key = jax.random.key(seed)
        k_w, k_t = jax.random.split(key)
        weight = jax.random.truncated_normal(k_w, -3.0, 3.0, (VOCAB, D_MODEL), dtype=jnp.float32)
        token_ids = jax.random.randint(k_t, (8, 1024), 0, VOCAB)
        return {'token_ids': token_ids, 'weight': weight}
    _L0_tok_all = _L0_tok_setup()
    _L0_tok_in = {k: v for k, v in _L0_tok_all.items() if k in ('weight',)}
    del _L0_tok_all

    def _L0_attn_setup():
        import jax, jax.numpy as jnp
        import numpy as np
        B, S, D = (2, 512, 256)
        H, HD = (16, 64)
        WIN = 64

        def _band_mask(seq_len, window):
            i = jnp.arange(seq_len)[:, None]
            j = jnp.arange(seq_len)[None, :]
            return (j > i) | (j < i - window)
        key = jax.random.key(seed)
        ks = jax.random.split(key, 9)
        scale = 0.02
        x = jax.random.normal(ks[0], (B, S, D), dtype=jnp.float32)
        Wq = jax.random.normal(ks[1], (D, H * HD), dtype=jnp.float32) * scale
        Wk = jax.random.normal(ks[2], (D, H * HD), dtype=jnp.float32) * scale
        Wv = jax.random.normal(ks[3], (D, H * HD), dtype=jnp.float32) * scale
        Wo = jax.random.normal(ks[4], (H * HD, D), dtype=jnp.float32) * scale
        bq = jnp.zeros((H * HD,), jnp.float32)
        bk = jnp.zeros((H * HD,), jnp.float32)
        bv = jnp.zeros((H * HD,), jnp.float32)
        bo = jnp.zeros((D,), jnp.float32)
        return {'x': x, 'Wq': Wq, 'bq': bq, 'Wk': Wk, 'bk': bk, 'Wv': Wv, 'bv': bv, 'Wo': Wo, 'bo': bo}
    _L0_attn_all = _L0_attn_setup()
    _L0_attn_in = {k: v for k, v in _L0_attn_all.items() if k in ('Wq', 'bq', 'Wk', 'bk', 'Wv', 'bv', 'Wo', 'bo')}
    del _L0_attn_all

    def _L0_ffn_setup():
        import jax, jax.numpy as jnp
        import numpy as np
        from functools import partial
        HEADS = 16
        EPS = 1e-12

        def _l2_normalize(z):
            n = jnp.linalg.norm(z, axis=-1, keepdims=True)
            return z / jnp.maximum(n, EPS)
        key = jax.random.key(seed)
        kx, kq, kk, kv, ko, kf = jax.random.split(key, 6)
        B, S, D, L = (2, 512, 256, 256)
        scale = 0.02
        return {'x': jax.random.normal(kx, (B, S, D), dtype=jnp.float32), 'Wq': jax.random.normal(kq, (D, L), dtype=jnp.float32) * scale, 'Wk': jax.random.normal(kk, (D, L), dtype=jnp.float32) * scale, 'Wv': jax.random.normal(kv, (D, L), dtype=jnp.float32) * scale, 'Wo': jax.random.normal(ko, (L, D), dtype=jnp.float32) * scale, 'Wff': jax.random.normal(kf, (D, D), dtype=jnp.float32) * scale}
    _L0_ffn_all = _L0_ffn_setup()
    _L0_ffn_in = {k: v for k, v in _L0_ffn_all.items() if k in ('Wq', 'Wk', 'Wv', 'Wo', 'Wff')}
    del _L0_ffn_all
    return {'x': x, 'L0_tok_weight': _L0_tok_in['weight'], 'L0_attn_Wq': _L0_attn_in['Wq'], 'L0_attn_bq': _L0_attn_in['bq'], 'L0_attn_Wk': _L0_attn_in['Wk'], 'L0_attn_bk': _L0_attn_in['bk'], 'L0_attn_Wv': _L0_attn_in['Wv'], 'L0_attn_bv': _L0_attn_in['bv'], 'L0_attn_Wo': _L0_attn_in['Wo'], 'L0_attn_bo': _L0_attn_in['bo'], 'L0_ffn_Wq': _L0_ffn_in['Wq'], 'L0_ffn_Wk': _L0_ffn_in['Wk'], 'L0_ffn_Wv': _L0_ffn_in['Wv'], 'L0_ffn_Wo': _L0_ffn_in['Wo'], 'L0_ffn_Wff': _L0_ffn_in['Wff']}

def reference(x, L0_tok_weight, L0_attn_Wq, L0_attn_bq, L0_attn_Wk, L0_attn_bk, L0_attn_Wv, L0_attn_bv, L0_attn_Wo, L0_attn_bo, L0_ffn_Wq, L0_ffn_Wk, L0_ffn_Wv, L0_ffn_Wo, L0_ffn_Wff):
    import jax
    import jax.numpy as jnp

    def _L0_tok_ref(token_ids, weight):
        import jax, jax.numpy as jnp
        import numpy as np
        VOCAB = 50257
        D_MODEL = 256
        return weight[token_ids]

    def _L0_attn_ref(x, Wq, bq, Wk, bk, Wv, bv, Wo, bo):
        import jax, jax.numpy as jnp
        import numpy as np
        B, S, D = (2, 512, 256)
        H, HD = (16, 64)
        WIN = 64

        def _band_mask(seq_len, window):
            i = jnp.arange(seq_len)[:, None]
            j = jnp.arange(seq_len)[None, :]
            return (j > i) | (j < i - window)
        b, s, _ = x.shape
        q = (x @ Wq + bq).reshape(b, s, H, HD)
        k = (x @ Wk + bk).reshape(b, s, H, HD)
        v = (x @ Wv + bv).reshape(b, s, H, HD)
        scores = jnp.einsum('bihd,bjhd->bhij', q, k) / jnp.sqrt(jnp.float32(HD))
        mask = _band_mask(s, WIN)
        scores = jnp.where(mask[None, None, :, :], -jnp.inf, scores)
        attn = jax.nn.softmax(scores, axis=-1)
        out = jnp.einsum('bhij,bjhd->bihd', attn, v).reshape(b, s, H * HD)
        return out @ Wo + bo

    def _L0_ffn_ref(x, Wq, Wk, Wv, Wo, Wff):
        import jax, jax.numpy as jnp
        import numpy as np
        from functools import partial
        HEADS = 16
        EPS = 1e-12

        def _l2_normalize(z):
            n = jnp.linalg.norm(z, axis=-1, keepdims=True)
            return z / jnp.maximum(n, EPS)
        B, S, D = x.shape
        H = HEADS
        L = Wq.shape[1]
        dh = L // H

        def split_heads(t):
            return t.reshape(B, S, H, dh).transpose(0, 2, 1, 3).reshape(B * H, S, dh)
        q = split_heads(x @ Wq)
        k = split_heads(x @ Wk)
        v = split_heads(x @ Wv)
        scores = jnp.einsum('bqd,bkd->bkq', q, k) / jnp.sqrt(jnp.asarray(D, x.dtype))
        attn = jax.nn.softmax(scores, axis=-1)
        out = jnp.einsum('bkq,bkv->bqv', attn, v)
        z = out.reshape(B, H, S, dh).transpose(0, 2, 1, 3).reshape(B, S, L)
        z = z @ Wo
        z = _l2_normalize(z)
        z = z @ Wff
        z = _l2_normalize(z)
        z = jax.nn.gelu(z, approximate=False)
        return z
    h = _L0_tok_ref(x, L0_tok_weight)
    h = h + _L0_attn_ref(_layernorm(h, axis=-1), L0_attn_Wq, L0_attn_bq, L0_attn_Wk, L0_attn_bk, L0_attn_Wv, L0_attn_bv, L0_attn_Wo, L0_attn_bo)
    h = h + _L0_ffn_ref(_layernorm(h, axis=-1), L0_ffn_Wq, L0_ffn_Wk, L0_ffn_Wv, L0_ffn_Wo, L0_ffn_Wff)
    return h

_drawn_inputs = setup_inputs


def setup_inputs(seed=0):
    import zlib

    import numpy as np

    out = dict(_drawn_inputs(seed))
    spreads = {'L0_attn_bq': (0.0, 0.8),
     'L0_attn_bk': (0.0, 0.8),
     'L0_attn_bv': (0.0, 0.1),
     'L0_attn_bo': (0.0, 0.1)}
    factors = {'L0_attn_Wq': 8.0, 'L0_attn_Wk': 8.0, 'L0_ffn_Wq': 8.0, 'L0_ffn_Wk': 8.0}
    for name, (base, spread) in spreads.items():
        noise = np.random.default_rng([zlib.crc32(name.encode()), seed]).standard_normal(out[name].shape)
        drawn = base * np.exp(spread * noise) if base else spread * noise
        out[name] = jnp.asarray(drawn.astype(out[name].dtype))
    for name, factor in factors.items():
        out[name] = (out[name] * factor).astype(out[name].dtype)
    return out
```

```python
import concourse.bass as bass
from concourse import mybir
from contextlib import ExitStack

F32 = mybir.dt.float32
F16 = mybir.dt.float16
BF16 = mybir.dt.bfloat16
I32 = mybir.dt.int32
ALU = mybir.AluOpType
ACT = mybir.ActivationFunctionType
AX = mybir.AxisListType


def tower_kernel(nc, tok, table, wq, bq, wk, bk, wv, bv, wo, bo, wq2, wk2, wv2, wo2, wff, out):
    P = 128
    NSEQ = out.shape[0]
    D = table.shape[1]
    DC = D // P
    H = 16
    HD = wq.shape[1] // H
    HC = wq.shape[1] // P
    G = 4
    NG = H // G
    T = 4
    U = T * NG
    NQUAD = NSEQ // T
    N = T * P
    VW = HD + 2
    DH2 = D // H
    H8 = P // DH2
    WIN = 64
    WS = 64.0
    HALF = P // 2
    PICK = 2.0 ** 15
    SCALE1 = 1.0 / (HD ** 0.5) / (WS * WS)
    SCALE2 = 1.0 / (D ** 0.5) / (WS * WS)
    UNSCALE = 1.0 / (WS * WS)
    LN_EPS = 1e-5
    L2_EPS = 1e-12
    MASKED = -1e30

    V0 = U + 1
    LAST = V0 + U + 6
    PR = 2 * HC + 2 * T
    P3_JOBS = [(4 * t + 11 + e, w, t) for t in range(T) for e, w in enumerate(("x2", "qk2", "v2"))]
    XN_JOBS = [((8, 9, 10, 14)[t], "xn", t) for t in range(T)]
    REPEAT = V0 + 20
    LATE = 6
    P1_SLOTS = [V0 + x for x in (1, 2, 4, 5, 6, 8, 9, 10, 11, 12, 13, 14, 15, 16, 17, 18, 20, 21)]
    P1_JOBS = [(P1_SLOTS[j], "p1", j) for j in range(PR - LATE)]
    LATE_JOBS = [(j, "late", PR - LATE + j) for j in range(LATE)]
    T_JOBS = [(u + 5, "o", u) for u in range(U)] + [(V0 + 4 * t + 8, "z", t) for t in range(T)]
    P_JOBS = [sorted(x, key=lambda job: job[0]) for x in (LATE_JOBS + XN_JOBS + P3_JOBS + P1_JOBS, LATE_JOBS + P3_JOBS)]
    NPJ, NTJ = len(P_JOBS[False]), len(T_JOBS)
    PRO = T + PR - LATE

    def p_bank(last, n):
        if P_JOBS[last][n][0] < V0:
            return 0
        return (NPJ - 1 - n + (P_JOBS[last][n][0] < REPEAT)) % 2

    def p_before(last, n):
        same = [m for m in range(n) if p_bank(last, m) == p_bank(last, n)]
        return same[-1] if same else None

    ctx = ExitStack()
    with ctx:
        def sb(name, shape, dt):
            return ctx.enter_context(nc.sbuf_tensor(name, shape, dt))

        def sem(name):
            return ctx.enter_context(nc.semaphore(name))

        w1_hi = sb("w1_hi", [P, 3, DC, H * HD], F16)
        w1_lo = sb("w1_lo", [P, 3, DC, H * HD], F16)
        wo_hi = sb("wo_hi", [P, HC, D], F16)
        wo_lo = sb("wo_lo", [P, HC, D], F16)
        w2_hi = sb("w2_hi", [P, 3, DC, D], F16)
        w2_lo = sb("w2_lo", [P, 3, DC, D], F16)
        wf_hi = sb("wf_hi", [P, DC, 2 * D], F16)
        wf_lo = sb("wf_lo", [P, DC, 2 * D], F16)
        bias_qk = sb("bias_qk", [P, 2, HC], F32)
        bv_col = sb("bv_col", [P, HC], F32)
        c_all = sb("c_all", [P, D], F32)
        ones_row = sb("ones_row", [1, P], F32)
        ident = sb("ident", [P, P], F32)
        ident_b = sb("ident_b", [P, P], BF16)
        band = sb("band", [P, G, P], BF16)
        pick = sb("pick", [P, G, P], BF16)
        pow_half = sb("pow_half", [P, T], F32)

        idx = sb("idx", [P, T], I32)
        rows = sb("rows", [P, T, D], F32)
        xn = sb("xn", [P, T, D], F32)
        res1 = sb("res1", [P, T, D], F32)
        h2 = sb("h2", [P, T, D], F32)
        x2 = sb("x2", [P, T, D], F32)
        st6 = sb("st6", [P, 2, T, 6], F32)
        mv = sb("mv", [P, 2, T, 2], F32)
        rstd = sb("rstd", [P, 2, T], F32)
        xT_hi = sb("xT_hi", [P, DC, N], F16)
        xT_lo = sb("xT_lo", [P, DC, N], F16)
        x2T_hi = sb("x2T_hi", [P, DC, P], F16)
        x2T_lo = sb("x2T_lo", [P, DC, P], F16)
        qz_hi = sb("qz_hi", [P, HC, T, 2, P], F16)
        qz_lo = sb("qz_lo", [P, HC, T, 2, P], F16)
        k_hi = sb("k_hi", [P, HC, N], F16)
        k_lo = sb("k_lo", [P, HC, N], F16)
        v_hi = sb("v_hi", [P, T, H, VW], F16)
        v_lo = sb("v_lo", [P, T, H, VW], F16)
        neg_max = sb("neg_max", [P, 2, G], BF16)
        maxT = sb("maxT", [P, 2, P], BF16)
        e_f = sb("e_f", [P, 2, G * P], F32)
        e_hi = sb("e_hi", [P, 3, G * P], F16)
        e_lo = sb("e_lo", [P, 3, G * P], F16)
        rsum = sb("rsum", [P, 2, G], F32)
        o_f = sb("o_f", [P, 2, G * HD], F32)
        oT_hi = sb("oT_hi", [P, 2, G * HD], F16)
        oT_lo = sb("oT_lo", [P, 2, G * HD], F16)
        q2_hilo = sb("q2_hilo", [P, 2, 2, DC, P], F16)
        q2z = sb("q2z", [P, 2, 2, DC, H8, P], F16)
        k2_hl = sb("k2_hl", [P, T, DC, 2, P], F16)
        k2_hm = sb("k2_hm", [HALF + G, T, DC, 2, P], F16)
        v2 = sb("v2", [P, T, D], F32)
        f_hi = sb("f_hi", [P, 2, NG, G * P], F16)
        f_lo = sb("f_lo", [P, 2, NG, G * P], F16)
        sum2 = sb("sum2", [P, 2, H], F32)
        rsum2 = sb("rsum2", [P, 2, H], F32)
        v2n = sb("v2n", [P, D], F32)
        v2n_hi = sb("v2n_hi", [P, D], F16)
        v2n_lo = sb("v2n_lo", [P, D], F16)
        z_f = sb("z_f", [P, D], F32)
        zT_hi = sb("zT_hi", [P, D], F16)
        zT_lo = sb("zT_lo", [P, D], F16)
        z2 = x2
        square = sb("square", [P, 2, D], F32)
        ss = sb("ss", [P, 2, T], F32)
        inv = sb("inv", [P, 2, T], F32)
        y = sb("y", [P, T, D], F32)

        c_row, bo_row = z_f[0:1, :], v2n[0:1, :]

        def flat32(x, pattern):
            return x.rearrange(pattern).bitcast(F32)

        in_q2z = flat32(q2z[:], "p b a c h n -> p (b a c h n)")
        in_qz_hi = flat32(qz_hi[:], "p c t h n -> p (c t h n)")
        in_qz_lo = flat32(qz_lo[:], "p c t h n -> p (c t h n)")
        st_w1 = [x.rearrange("p (c n) -> p c n", c=DC) for x in
                 (in_q2z[:, 0:2048], in_q2z[:, 2048:4096], flat32(k_hi[:], "p c n -> p (c n)"))]
        st_wo = flat32(k_lo[:], "p c n -> p (c n)").rearrange("p (c n) -> p c n", c=HC)
        st_w2 = [in_qz_hi[:, i * 512:(i + 1) * 512].rearrange("p (c n) -> p c n", c=DC) for i in range(3)]
        st_wo2 = in_qz_hi[:, 1536:2048].rearrange("p (c n) -> p c n", c=DC)
        st_wff, wo2T, st_wf = [in_qz_lo[:, i * 512:(i + 1) * 512].rearrange("p (c n) -> p c n", c=DC)
                               for i in range(3)]

        bank = [ctx.enter_context(nc.psum_tensor(f"bank{i}", [P, 512], F32)) for i in range(7)]
        SM, PB, ST, PV, TB, WO = bank[0], [bank[1], bank[0]], bank[2:4], bank[4], bank[5], bank[6]
        MT = ctx.enter_context(nc.psum_tensor("bank_mt", [P, 1024], BF16))

        w_in = sem("w_in")
        w_split = sem("w_split")
        w_tmp = sem("w_tmp")
        w_ps = sem("w_ps")
        w_bias = sem("w_bias")
        consts = sem("consts")
        cstep = sem("cstep")
        zeroed = sem("zeroed")
        picked = sem("picked")
        pool_past = sem("pool_past")
        dve_past = sem("dve_past")
        sp_past = sem("sp_past")
        idx_in = sem("idx_in")
        gathered = sem("gathered")
        res1_ok = sem("res1_ok")
        ln1_st = sem("ln1_st")
        ln1_mv = sem("ln1_mv")
        ln1_eps = sem("ln1_eps")
        ln1_rs = sem("ln1_rs")
        xn_ok = sem("xn_ok")
        t_ps = sem("t_ps")
        t_hi = sem("t_hi")
        t_lo = sem("t_lo")
        p_ps = sem("p_ps")
        p_hi = sem("p_hi")
        p_lo = sem("p_lo")
        sm_ps = sem("sm_ps")
        m_neg = sem("m_neg")
        m_ps = sem("m_ps")
        m_sb = sem("m_sb")
        st_ps = sem("st_ps")
        e_exp = sem("e_exp")
        e_msk0 = sem("e_msk0")
        e_msk = sem("e_msk")
        e_h = sem("e_h")
        e_l = sem("e_l")
        pv_ps = sem("pv_ps")
        o_r = sem("o_r")
        o_ok = sem("o_ok")
        wo_ps = sem("wo_ps")
        h2_ok = sem("h2_ok")
        ln2_st = sem("ln2_st")
        ln2_mv = sem("ln2_mv")
        ln2_eps = sem("ln2_eps")
        ln2_rs = sem("ln2_rs")
        x2_ok = sem("x2_ok")
        q2z_in = [[sem(f"q2z_in{b}{e}") for e in range(2)] for b in range(2)]
        s2_ps = sem("s2_ps")
        s2m_ps = sem("s2m_ps")
        f_exp = sem("f_exp")
        f_h = sem("f_h")
        f_l = sem("f_l")
        f_sum = sem("f_sum")
        r2_ok = sem("r2_ok")
        v2n_ok = sem("v2n_ok")
        v2n_h = sem("v2n_h")
        v2n_l = sem("v2n_l")
        z_ps = sem("z_ps")
        z_sb = sem("z_sb")
        wf_ps = sem("wf_ps")
        z2_ok = sem("z2_ok")
        nrm = sem("nrm")
        y_ok = sem("y_ok")
        gelu_ok = sem("gelu_ok")
        out_sum = sem("out_sum")
        stored = sem("stored")

        out_q = out.rearrange("b s d -> s b d")

        def ge(eng, s, value):
            if not isinstance(value, int) or value > 0:
                eng.wait_ge(s, value)

        def q2z_count(it, t):
            return it * (16 * G * T) + 32 * G * (t // 2 + 1)

        def t_count(it, n):
            return it * NTJ + (n + 1)

        def p_count(it, n):
            return it * NPJ + (PRO + n + 1)

        def p_hi_count(it, last, n):
            return it * (NPJ - T) + (PRO + n + 1 - sum(w == "v2" for _, w, _ in P_JOBS[last][:n + 1]))

        def quads(nc_engine, body):
            body(0, True, False)
            with nc_engine.Fori(1, NQUAD - 1) as it:
                body(it, False, False)
            body(NQUAD - 1, False, True)

        def t_jobs(s, what):
            return [(n, w, i) for n, (at, w, i) in enumerate(T_JOBS) if (at, w) == (s, what)]

        def t_job_of(it, w, i):
            return t_count(it, [x[1:] for x in T_JOBS].index((w, i)))

        def p_job_of(it, last, w, i):
            return p_count(it, [x[1:] for x in P_JOBS[last]].index((w, i)))

        def p_jobs(s, last):
            return [(n, w, i) for n, (at, w, i) in enumerate(P_JOBS[last]) if at == s]

        NORMED_SLOT = 5
        Z_SLOT = {V0 + 4 * t + 7: t for t in range(T)}
        WF_SLOT = {V0 + 4 * t + 9: t for t in range(T)}
        V2N_SLOT = {V0 + 4 * t + 5: t for t in range(T)}

        block = ctx.enter_context(nc.Block())


        @block.sync
        def _(sp):
            for i, w in enumerate((wq, wk, wv)):
                sp.dma_start(st_w1[i], w.rearrange("(c p) n -> p c n", p=P)).then_inc(w_in, 16)
            sp.dma_start(st_wo, wo.rearrange("(c p) n -> p c n", p=P)).then_inc(w_in, 16)
            for i, w in enumerate((wq2, wk2, wv2)):
                sp.dma_start(st_w2[i], w.rearrange("(c p) n -> p c n", p=P)).then_inc(w_in, 16)
            sp.dma_start(st_wo2, wo2.rearrange("(c p) n -> p c n", p=P)).then_inc(w_in, 16)
            sp.dma_start(st_wff, wff.rearrange("(c p) n -> p c n", p=P)).then_inc(w_in, 16)
            with nc.allow_non_contiguous_dma(reason="biases, once"):
                for i, b in enumerate((bq, bk)):
                    sp.dma_start(bias_qk[:, i, :], b.rearrange("(c p) -> p c", p=P)).then_inc(w_in, 16)
                sp.dma_start(bv_col[:], bv.rearrange("(c p) -> p c", p=P)).then_inc(w_in, 16)
            sp.dma_start(bo_row[:], bo.rearrange("(a n) -> a n", a=1)).then_inc(w_in, 16)
            sp.dma_start(idx[:], tok[:, 0:T]).then_inc(idx_in, 16)

            def store(n):
                sp.wait_ge(out_sum, n + 1)
                sp.sem_inc(sp_past, 1)
                sp.dma_start(out_q[:, bass.ds(n * T, T), :], y[:]).then_inc(stored, 16)

            def quad(it, first, last):
                if not last:
                    sp.wait_ge(gathered, it * (16 * T) + 16 * T)
                    sp.sem_inc(sp_past, 1)
                    sp.dma_start(idx[:], tok[:, bass.ds(it * T + T, T)]).then_inc(idx_in, 16)
                if not first:
                    store(it - 1)
                for n, (_, w, t) in enumerate(P_JOBS[last]):
                    if w == "qk2":
                        sp.wait_ge(p_lo, p_count(it, n))
                        sp.sem_inc(sp_past, 1)
                        ge(sp, s2m_ps, it * U + (t - 1) * NG)
                        for h in range(H8):
                            r = slice(h * DH2, (h + 1) * DH2)
                            k = h % G * DH2
                            sp.dma_start(q2z[k:k + DH2, t % 2, :, :, h, :].rearrange("p a c n -> p (a c) n"),
                                         q2_hilo[r, t % 2].rearrange("p a c n -> p (a c) n")).then_inc(q2z_in[t % 2][h // G], 16)
                            sp.dma_start(q2z[HALF + k:HALF + k + DH2, t % 2, 0, :, h, :],
                                         q2_hilo[r, t % 2, 0]).then_inc(q2z_in[t % 2][h // G], 16)

            quads(nc.sync, quad)
            store(NQUAD - 1)
            sp.wait_ge(stored, 16 * NQUAD)

        @block.gpsimd
        def _(pool):
            nc.gpsimd.memset(ident[:], 0.0).then_inc(cstep, 1)
            nc.gpsimd.memset(pick[:], 0.0).then_inc(cstep, 1)
            nc.gpsimd.memset(band[:], 0.0).then_inc(cstep, 1)
            pool.wait_ge(cstep, 3)
            nc.gpsimd.affine_select(out=ident[:], in_=ident[:], compare_op=ALU.not_equal, fill=1.0, base=0,
                                    pattern=[[-1, P]], channel_multiplier=1).then_inc(cstep, 1)
            nc.gpsimd.affine_select(out=pick[:], in_=pick[:], compare_op=ALU.not_equal, fill=1.0, base=0,
                                    pattern=[[-1, G], [0, P]], channel_multiplier=1).then_inc(consts, 1)
            nc.gpsimd.affine_select(out=band[:], in_=band[:], compare_op=ALU.is_ge, fill=MASKED, base=0,
                                    pattern=[[0, G], [-1, P]], channel_multiplier=1).then_inc(cstep, 1)
            pool.wait_ge(cstep, 5)
            nc.gpsimd.affine_select(out=band[:], in_=band[:], compare_op=ALU.is_ge, fill=MASKED, base=WIN,
                                    pattern=[[0, G], [1, P]], channel_multiplier=-1).then_inc(consts, 1)
            nc.gpsimd.tensor_copy(ident_b[:], ident[:]).then_inc(consts, 1)
            nc.gpsimd.memset(pow_half[:], -0.5).then_inc(consts, 1)
            nc.gpsimd.memset(maxT[:], 0.0).then_inc(consts, 1)
            nc.gpsimd.memset(ones_row[:], 1.0).then_inc(consts, 1)
            nc.gpsimd.memset(v_lo[:, :, :, HD:VW], 0.0).then_inc(consts, 1)
            nc.gpsimd.memset(v_hi[:, :, :, HD:HD + 1], 1.0).then_inc(consts, 1)
            nc.gpsimd.memset(v_hi[:, :, :, HD + 1:VW], 0.0).then_inc(consts, 1)

            def gather(n):
                pool.wait_ge(idx_in, n * 16 + 16)
                pool.sem_inc(pool_past, 1)
                for t in range(T):
                    nc.gpsimd.indirect_dma_start(
                        out=rows[:, t, :], out_offset=None, in_=table[:, :],
                        in_offset=bass.IndirectOffsetOnAxis(ap=idx[:, t:t + 1], axis=0)).then_inc(gathered, 16)

            def ln1_root(n):
                pool.wait_ge(ln1_eps, n + 1)
                nc.gpsimd.tensor_tensor(rstd[:, 0, :], rstd[:, 0, :], pow_half[:], ALU.pow).then_inc(ln1_rs, 1)

            def residual(n):
                pool.wait_ge(gathered, n * (16 * T) + 16 * T)
                ge(pool, h2_ok, n * T)
                nc.gpsimd.tensor_tensor(res1[:], rows[:], c_all[:].unsqueeze(1).broadcast_to([P, T, D]),
                                        ALU.add).then_inc(res1_ok, 1)

            def norms(n, part):
                if part == 0:
                    pool.wait_ge(z2_ok, n * (3 * T) + 3 * T)
                    pool.sem_inc(pool_past, 1)
                    nc.gpsimd.tensor_scalar(inv[:, 0], ss[:, 0], (L2_EPS * WS * WS) ** 2, None,
                                            ALU.max).then_inc(nrm, 1)
                    pool.wait_ge(nrm, n * 6 + 1)
                    nc.gpsimd.tensor_tensor(inv[:, 0], inv[:, 0], pow_half[:], ALU.pow).then_inc(nrm, 1)
                elif part == 1:
                    pool.wait_ge(nrm, n * 6 + 2)
                    nc.gpsimd.tensor_tensor(ss[:, 1], ss[:, 1], inv[:, 0], ALU.mult).then_inc(nrm, 1)
                    pool.wait_ge(nrm, n * 6 + 3)
                    nc.gpsimd.tensor_tensor(ss[:, 1], ss[:, 1], inv[:, 0], ALU.mult).then_inc(nrm, 1)
                else:
                    pool.wait_ge(nrm, n * 6 + 4)
                    pool.sem_inc(pool_past, 1)
                    nc.gpsimd.tensor_scalar(inv[:, 1], ss[:, 1], L2_EPS ** 2, None, ALU.max).then_inc(nrm, 1)
                    pool.wait_ge(nrm, n * 6 + 5)
                    nc.gpsimd.tensor_tensor(inv[:, 1], inv[:, 1], pow_half[:], ALU.pow).then_inc(nrm, 1)

            gather(0)
            pool.wait_ge(w_split, 18)
            nc.gpsimd.memset(qz_hi[:], 0.0).then_inc(zeroed, 1)
            nc.gpsimd.memset(qz_lo[:], 0.0).then_inc(zeroed, 1)
            nc.gpsimd.memset(q2z[:], 0.0).then_inc(zeroed, 1)
            pool.wait_ge(w_bias, 5)
            ln1_root(0)
            residual(0)

            def quad(it, first, last):
                for s in range(LAST):
                    if s == 0 and not last:
                        pool.wait_ge(xn_ok, it * T + T)
                        pool.wait_ge(res1_ok, it + 1)
                        gather(it + 1)
                    u = s - 1
                    if 0 <= u < U:
                        pool.wait_ge(e_exp, it * U + (u + 1))
                        pool.sem_inc(pool_past, 1)
                        ef = e_f[:, u % 2].rearrange("p (g n) -> p g n", g=G)
                        nc.gpsimd.affine_select(out=ef, in_=ef, compare_op=ALU.is_ge, fill=0.0, base=0,
                                                pattern=[[0, G], [1, P]], channel_multiplier=-1).then_inc(e_msk0, 1)
                        pool.wait_ge(e_msk0, it * U + (u + 1))
                        pool.sem_inc(pool_past, 1)
                        eh = ef[:, :, WIN:P]
                        nc.gpsimd.affine_select(out=eh, in_=eh, compare_op=ALU.is_ge, fill=0.0, base=0,
                                                pattern=[[0, G], [-1, P - WIN]], channel_multiplier=1
                                                ).then_inc(e_msk, 1)
                    u = s - 2
                    if 0 <= u < U:
                        pool.wait_ge(e_h, it * U + (u + 1))
                        ge(pool, pv_ps, it * U + (u - 2))
                        nc.gpsimd.tensor_tensor(e_lo[:, u % 3], e_f[:, u % 2], e_hi[:, u % 3],
                                                ALU.subtract).then_inc(e_l, 1)
                    if 1 <= s <= 3 and not first:
                        norms(it - 1, s - 1)
                    if s == 5 and not last:
                        ln1_root(it + 1)
                    u = s - 6
                    if 0 <= u < U and u % NG == NG - 1:
                        t = u // NG
                        pool.wait_ge(ln2_eps, it * T + (t + 1))
                        nc.gpsimd.tensor_tensor(rstd[:, 1, t:t + 1], rstd[:, 1, t:t + 1], pow_half[:, 0:1],
                                                ALU.pow).then_inc(ln2_rs, 1)
                    v = s - V0 - 2
                    if 0 <= v < U:
                        t, g = v // NG, v % NG
                        pool.wait_ge(f_h, it * U + (v + 1))
                        nc.gpsimd.tensor_tensor(f_lo[:, t % 2, g], e_f[:, v % 2], f_hi[:, t % 2, g],
                                                ALU.subtract).then_inc(f_l, 1)
                    if s == V0 + 6 and not last:
                        residual(it + 1)

            quads(nc.gpsimd, quad)
            for part in range(3):
                norms(NQUAD - 1, part)

        @block.scalar
        def _(act):
            act.wait_ge(w_in, 16 * 13)
            for i in range(3):
                nc.scalar.activation(w1_hi[:, i], st_w1[i], ACT.Copy, scale=WS).then_inc(w_tmp, 1)
            nc.scalar.activation(wo_hi[:], st_wo, ACT.Copy, scale=WS).then_inc(w_tmp, 1)
            for i in range(3):
                nc.scalar.activation(w2_hi[:, i], st_w2[i], ACT.Copy, scale=WS).then_inc(w_tmp, 1)
            nc.scalar.activation(wf_hi[:, :, 0:D], st_wo2, ACT.Copy, scale=WS).then_inc(w_tmp, 1)
            nc.scalar.activation(bias_qk[:], bias_qk[:], ACT.Copy, scale=WS).then_inc(w_bias, 1)
            act.wait_ge(w_ps, 3)
            for c in range(DC):
                nc.scalar.activation(st_wf[:, c], bank[2 + c][:, 0:D], ACT.Copy).then_inc(w_bias, 1)
            act.wait_ge(w_bias, 3)
            nc.scalar.activation(wf_hi[:, :, D:2 * D], st_wf, ACT.Copy, scale=WS).then_inc(w_tmp, 1)

            def transposed(b, w, i):
                if w in ("xn", "x2"):
                    dst = xT_hi[:, :, i * P:(i + 1) * P] if w == "xn" else x2T_hi[:]
                    nc.scalar.activation(dst, b[:, 0:D].rearrange("p (c n) -> p c n", c=DC),
                                         ACT.Copy).then_inc(p_hi, 1)
                else:
                    dst = oT_hi[:, i % 2] if w == "o" else zT_hi[:]
                    nc.scalar.activation(dst, b[:, 0:D], ACT.Copy).then_inc(t_hi, 1)

            def projected(b, j):
                if j < HC:
                    nc.scalar.activation(k_hi[:, j], b[:], ACT.Identity,
                                         bias=bias_qk[:, 1, j:j + 1]).then_inc(p_hi, 1)
                elif j < 2 * HC:
                    c = j - HC
                    for e in range(2):
                        r = slice(e * HD, (e + 1) * HD)
                        half = nc.scalar.activation(qz_hi[r, c, :, e, :], b[r, :].rearrange("p (t n) -> p t n", t=T),
                                                    ACT.Identity, bias=bias_qk[r, 0, c:c + 1])
                    half.then_inc(p_hi, 1)
                else:
                    t, e = (j - 2 * HC) // 2, j % 2
                    nc.scalar.activation(v_hi[:, t, e * 8:(e + 1) * 8, 0:HD],
                                         b[:].rearrange("p (h d) -> p h d", d=HD), ACT.Copy).then_inc(p_hi, 1)

            act.wait_ge(consts, 9)
            act.wait_ge(zeroed, 3)
            for b in range(2):
                for c in range(DC):
                    for e in range(2):
                        nc.scalar.activation(q2z[HALF:HALF + G, b, 1, c, e * G:(e + 1) * G], pick[0:G], ACT.Copy,
                                             scale=PICK).then_inc(picked, 1)
            for t in range(T):
                act.wait_ge(p_ps, t + 1)
                transposed(PB[(t + 1) % 2], "xn", t)
            for j in range(PR - LATE):
                act.wait_ge(p_ps, T + j + 1)
                projected(PB[(j + 1) % 2], j)

            def gelu(n):
                act.wait_ge(y_ok, n * T + T)
                nc.scalar.activation(y[:], y[:], ACT.Gelu).then_inc(gelu_ok, 1)

            def quad(it, first, last):
                for s in range(LAST):
                    u = s - 1
                    if 0 <= u < U:
                        act.wait_ge(m_ps, it * (2 * U) + (u + 1))
                        nc.scalar.activation(maxT[0:G, u % 2], MT[0:G, 0:P], ACT.Copy).then_inc(m_sb, 1)
                    v = s - V0 - 1
                    if 0 <= v < U:
                        act.wait_ge(m_ps, it * (2 * U) + (U + v + 1))
                        nc.scalar.activation(k2_hm[HALF:HALF + G, v // NG, (v % NG) // 2, v % 2], MT[0:G, 0:P],
                                             ACT.Copy, scale=1.0 / PICK).then_inc(m_sb, 1)
                    if s - 1 in V2N_SLOT:
                        t = V2N_SLOT[s - 1]
                        act.wait_ge(v2n_ok, it * T + (t + 1))
                        nc.scalar.activation(v2n_hi[:], v2n[:], ACT.Copy).then_inc(v2n_h, 1)
                    v = s - V0 - 2
                    if 0 <= v < U:
                        t, g = v // NG, v % NG
                        act.wait_ge(f_exp, it * U + (v + 1))
                        nc.scalar.activation(f_hi[:, t % 2, g], e_f[:, v % 2], ACT.Copy).then_inc(f_h, 1)
                    for n, w, i in t_jobs(s, "o"):
                        act.wait_ge(t_ps, t_count(it, n))
                        transposed(TB, w, i)
                    u = s - 1
                    if 0 <= u < U:
                        act.wait_ge(st_ps, it * U + (u + 1))
                        ge(act, e_l, it * U + (u - 1))
                        if u < 2:
                            ge(act, f_l, it * U)
                            ge(act, f_sum, it * U)
                        nc.scalar.activation(e_f[:, u % 2], ST[u % 2][:], ACT.Exp, scale=SCALE1).then_inc(e_exp, 1)
                    u = s - 2
                    if 0 <= u < U:
                        act.wait_ge(e_msk, it * U + (u + 1))
                        ge(act, pv_ps, it * U + (u - 2))
                        nc.scalar.activation(e_hi[:, u % 3], e_f[:, u % 2], ACT.Copy).then_inc(e_h, 1)
                    v = s - V0 - 1
                    if 0 <= v < U:
                        act.wait_ge(s2m_ps, it * U + (v + 1))
                        if v < 2:
                            act.wait_ge(e_l, it * U + U)
                        else:
                            act.wait_ge(f_l, it * U + (v - 1))
                            act.wait_ge(f_sum, it * U + (v - 1))
                        nc.scalar.activation(e_f[:, v % 2], ST[v % 2][:], ACT.Exp, scale=SCALE2).then_inc(f_exp, 1)
                    for n, w, i in t_jobs(s, "z"):
                        act.wait_ge(t_ps, t_count(it, n))
                        transposed(TB, w, i)
                    for n, w, i in p_jobs(s, last):
                        if w == "v2":
                            continue
                        act.wait_ge(p_ps, p_count(it, n))
                        b = PB[p_bank(last, n)]
                        if w in ("p1", "late"):
                            projected(b, i)
                        elif w != "qk2":
                            transposed(b, w, i)
                        else:
                            for e in range(2):
                                ge(act, q2z_in[i % 2][e], q2z_count(it, i) - 32 * G)
                            nc.scalar.activation(q2_hilo[:, i % 2, 0].rearrange("p c n -> p (c n)"), b[:, 0:D], ACT.Copy)
                            for e in range(2):
                                half = nc.scalar.activation(
                                    k2_hl[0:HALF, i, :, e], b[e * HALF:(e + 1) * HALF, D:2 * D].rearrange(
                                        "p (c n) -> p c n", c=DC), ACT.Copy)
                            half.then_inc(p_hi, 1)
                    if s in Z_SLOT:
                        act.wait_ge(z_ps, it * T + (Z_SLOT[s] + 1))
                        nc.scalar.activation(z_f[:], PV[:, 0:D], ACT.Copy).then_inc(z_sb, 1)
                    if s in WF_SLOT:
                        t = WF_SLOT[s]
                        act.wait_ge(wf_ps, it * T + (t + 1))
                        for e in range(2):
                            nc.scalar.activation(square[:, e], WO[:, e * D:(e + 1) * D], ACT.Square,
                                                 accum_out=ss[:, e, t:t + 1]).then_inc(z2_ok, 1)
                        nc.scalar.activation(z2[:, t], WO[:, D:2 * D], ACT.Copy).then_inc(z2_ok, 1)
                    if s == NORMED_SLOT + 2 and not first:
                        gelu(it - 1)

            quads(nc.scalar, quad)
            gelu(NQUAD - 1)

        @block.vector
        def _(dve):
            for n, (lo, st, hi) in enumerate(
                    [(w1_lo[:, i], st_w1[i], w1_hi[:, i]) for i in range(3)] + [(wo_lo[:], st_wo, wo_hi[:])]
                    + [(w2_lo[:, i], st_w2[i], w2_hi[:, i]) for i in range(3)]
                    + [(wf_lo[:, :, 0:D], st_wo2, wf_hi[:, :, 0:D])]):
                dve.wait_ge(w_tmp, n + 1)
                nc.vector.scalar_tensor_tensor(out=lo, in0=st, scalar=WS, in1=hi, op0=ALU.mult,
                                               op1=ALU.subtract).then_inc(w_split, 1)
            dve.wait_ge(w_ps, 1)
            for c in range(DC):
                nc.vector.tensor_copy(wo2T[:, c], bank[c][:, 0:D]).then_inc(w_split, 1)
            dve.wait_ge(w_tmp, 9)
            nc.vector.scalar_tensor_tensor(out=wf_lo[:, :, D:2 * D], in0=st_wf, scalar=WS, in1=wf_hi[:, :, D:2 * D],
                                           op0=ALU.mult, op1=ALU.subtract).then_inc(w_split, 7)
            dve.wait_ge(w_ps, 4)
            nc.vector.tensor_tensor(c_row[:], bank[4][0:1, 0:D], bo_row[:], ALU.add).then_inc(w_split, 1)
            dve.wait_ge(w_ps, 5)
            nc.vector.tensor_copy(c_all[:], bank[5][:, 0:D]).then_inc(w_bias, 2)

            def ln1(n, some):
                dve.wait_ge(gathered, n * (16 * T) + 16 * T)
                for t in some:
                    nc.vector.bn_stats(st6[:, 0, t], rows[:, t]).then_inc(ln1_st, 1)
                if some[-1] != T - 1:
                    return
                dve.wait_ge(ln1_st, n * T + T)
                dve.sem_inc(dve_past, 1)
                for t in range(T):
                    nc.vector.bn_aggr(mv[:, 0, t], st6[:, 0, t]).then_inc(ln1_mv, 1)
                dve.wait_ge(ln1_mv, n * T + T)
                nc.vector.tensor_scalar(rstd[:, 0], mv[:, 0, :, 1], LN_EPS, None, ALU.add).then_inc(ln1_eps, 1)

            def ln1_apply(n, some):
                dve.wait_ge(ln1_rs, n + 1)
                for t in some:
                    nc.vector.tensor_scalar(xn[:, t], rows[:, t], mv[:, 0, t, 0:1], rstd[:, 0, t:t + 1],
                                            ALU.subtract, ALU.mult).then_inc(xn_ok, 1)

            def transposed(b, w, i):
                if w in ("xn", "x2"):
                    at = slice(i * P, (i + 1) * P)
                    lo, hi = (xT_lo[:, :, at], xT_hi[:, :, at]) if w == "xn" else (x2T_lo[:], x2T_hi[:])
                    nc.vector.tensor_tensor(lo, b[:, 0:D].rearrange("p (c n) -> p c n", c=DC), hi,
                                            ALU.subtract).then_inc(p_lo, 1)
                else:
                    lo, hi = (oT_lo[:, i % 2], oT_hi[:, i % 2]) if w == "o" else (zT_lo[:], zT_hi[:])
                    nc.vector.tensor_tensor(lo, b[:, 0:D], hi, ALU.subtract).then_inc(t_lo, 1)

            def projected(b, j):
                if j < HC:
                    nc.vector.scalar_tensor_tensor(out=k_lo[:, j], in0=b[:], scalar=bias_qk[:, 1, j:j + 1],
                                                   in1=k_hi[:, j], op0=ALU.add, op1=ALU.subtract).then_inc(p_lo, 1)
                elif j < 2 * HC:
                    c = j - HC
                    for e in range(2):
                        r = slice(e * HD, (e + 1) * HD)
                        half = nc.vector.scalar_tensor_tensor(
                            out=qz_lo[r, c, :, e, :], in0=b[r, :].rearrange("p (t n) -> p t n", t=T),
                            scalar=bias_qk[r, 0, c:c + 1], in1=qz_hi[r, c, :, e, :], op0=ALU.add, op1=ALU.subtract)
                    half.then_inc(p_lo, 1)
                else:
                    t, e = (j - 2 * HC) // 2, j % 2
                    hs = slice(e * 8, (e + 1) * 8)
                    nc.vector.tensor_tensor(v_lo[:, t, hs, 0:HD], b[:].rearrange("p (h d) -> p h d", d=HD),
                                            v_hi[:, t, hs, 0:HD], ALU.subtract).then_inc(p_lo, 1)

            ln1(0, range(T))
            ln1_apply(0, range(T))
            dve.wait_ge(zeroed, 3)
            dve.wait_ge(consts, 9)
            for t in range(T):
                dve.wait_ge(p_hi, t + 1)
                transposed(PB[(t + 1) % 2], "xn", t)
            for j in range(PR - LATE):
                dve.wait_ge(p_hi, T + j + 1)
                projected(PB[(j + 1) % 2], j)

            def normed(n, some):
                dve.wait_ge(nrm, n * 6 + 6)
                ge(dve, stored, n * 16)
                for t in some:
                    nc.vector.tensor_scalar(y[:, t], z2[:, t], inv[:, 0, t:t + 1], inv[:, 1, t:t + 1],
                                            ALU.mult, ALU.mult).then_inc(y_ok, 1)

            def finish(n):
                dve.wait_ge(gelu_ok, n + 1)
                nc.vector.tensor_tensor(y[:], y[:], h2[:], ALU.add).then_inc(out_sum, 1)

            def quad(it, first, last):
                for s in range(LAST):
                    if s < U:
                        dve.wait_ge(sm_ps, it * U + (s + 1))
                        ge(dve, m_ps, it * (2 * U) + (s - 1))
                        nc.vector.tensor_reduce(out=neg_max[:, s % 2], in_=SM[:].rearrange(
                            "p (g n) -> p g n", g=G), op=ALU.max, axis=AX.X, negate=True).then_inc(m_neg, 1)
                    v = s - V0
                    if 0 <= v < U:
                        dve.wait_ge(s2_ps, it * U + (v + 1))
                        dve.wait_ge(m_ps, it * (2 * U) + (U + v - 1))
                        nc.vector.tensor_reduce(out=neg_max[:, v % 2], in_=ST[v % 2][:].rearrange(
                            "p (g n) -> p g n", g=G), op=ALU.max, axis=AX.X, negate=True).then_inc(m_neg, 1)
                    for n, w, i in t_jobs(s, "o"):
                        dve.wait_ge(t_hi, t_count(it, n))
                        transposed(TB, w, i)
                    v = s - V0 - 2
                    if 0 <= v < U:
                        t, g = v // NG, v % NG
                        dve.wait_ge(f_exp, it * U + (v + 1))
                        nc.vector.tensor_reduce(out=sum2[:, t % 2, g * G:(g + 1) * G], in_=e_f[:, v % 2].rearrange(
                            "p (g n) -> p g n", g=G), op=ALU.add, axis=AX.X).then_inc(f_sum, 1)
                    for n, w, i in t_jobs(s, "z"):
                        dve.wait_ge(t_hi, t_count(it, n))
                        transposed(TB, w, i)
                    u = s - 4
                    if 0 <= u < U:
                        dve.wait_ge(pv_ps, it * U + (u + 1))
                        pv = PV[:, 0:G * VW].rearrange("p (g d) -> p g d", d=VW)
                        nc.vector.reciprocal(rsum[:, u % 2], pv[:, :, HD]).then_inc(o_r, 1)
                        dve.wait_ge(o_r, it * U + (u + 1))
                        nc.vector.tensor_tensor(o_f[:, u % 2].rearrange("p (g d) -> p g d", d=HD), pv[:, :, 0:HD],
                                                rsum[:, u % 2].unsqueeze(2).broadcast_to([P, G, HD]),
                                                ALU.mult).then_inc(o_ok, 1)
                    u = s - 7
                    if 0 <= u < U and u % NG == NG - 1:
                        t = u // NG
                        dve.wait_ge(ln2_rs, it * T + (t + 1))
                        nc.vector.tensor_scalar(x2[:, t], h2[:, t], mv[:, 1, t, 0:1], rstd[:, 1, t:t + 1],
                                                ALU.subtract, ALU.mult).then_inc(x2_ok, 1)
                    u = s - 6
                    if 0 <= u < U and u % NG == NG - 1:
                        t = u // NG
                        dve.wait_ge(wo_ps, it * T + (t + 1))
                        if t == 0:
                            dve.wait_ge(res1_ok, it + 1)
                            ge(dve, out_sum, it)
                        nc.vector.scalar_tensor_tensor(out=h2[:, t], in0=WO[:, 0:D], scalar=UNSCALE, in1=res1[:, t],
                                                       op0=ALU.mult, op1=ALU.add).then_inc(h2_ok, 1)
                        dve.wait_ge(h2_ok, it * T + (t + 1))
                        nc.vector.bn_stats(st6[:, 1, t], h2[:, t]).then_inc(ln2_st, 1)
                        dve.wait_ge(ln2_st, it * T + (t + 1))
                        dve.sem_inc(dve_past, 1)
                        nc.vector.bn_aggr(mv[:, 1, t], st6[:, 1, t]).then_inc(ln2_mv, 1)
                        dve.wait_ge(ln2_mv, it * T + (t + 1))
                        nc.vector.tensor_scalar(rstd[:, 1, t:t + 1], mv[:, 1, t, 1:2], LN_EPS, None,
                                                ALU.add).then_inc(ln2_eps, 1)
                    if s in V2N_SLOT:
                        t = V2N_SLOT[s]
                        dve.wait_ge(f_sum, it * U + (t + 1) * NG)
                        nc.vector.reciprocal(rsum2[:, t % 2], sum2[:, t % 2]).then_inc(r2_ok, 1)
                        dve.wait_ge(r2_ok, it * T + (t + 1))
                        ge(dve, z_ps, it * T + t)
                        nc.vector.tensor_tensor(v2n[:].rearrange("p (h d) -> p h d", d=DH2),
                                                v2[:, t].rearrange("p (h d) -> p h d", d=DH2),
                                                rsum2[:, t % 2].unsqueeze(2).broadcast_to([P, H, DH2]),
                                                ALU.mult).then_inc(v2n_ok, 1)
                    if s - 1 in V2N_SLOT:
                        t = V2N_SLOT[s - 1]
                        dve.wait_ge(v2n_h, it * T + (t + 1))
                        nc.vector.tensor_tensor(v2n_lo[:], v2n[:], v2n_hi[:], ALU.subtract).then_inc(v2n_l, 1)
                    for n, w, i in p_jobs(s, last):
                        b = PB[p_bank(last, n)]
                        if w == "v2":
                            dve.wait_ge(p_ps, p_count(it, n))
                            nc.vector.tensor_copy(v2[:, i], b[:, 0:D]).then_inc(p_lo, 1)
                            continue
                        dve.wait_ge(p_hi, p_hi_count(it, last, n))
                        if w in ("p1", "late"):
                            projected(b, i)
                        elif w != "qk2":
                            transposed(b, w, i)
                        else:
                            nc.vector.tensor_tensor(q2_hilo[:, i % 2, 1].rearrange("p c n -> p (c n)"), b[:, 0:D],
                                                    q2_hilo[:, i % 2, 0].rearrange("p c n -> p (c n)"), ALU.subtract)
                            for e in range(2):
                                nc.vector.tensor_tensor(
                                    k2_hl[HALF:P, i, :, e], b[e * HALF:(e + 1) * HALF, D:2 * D].rearrange(
                                        "p (c n) -> p c n", c=DC), k2_hl[0:HALF, i, :, e], ALU.subtract)
                            nc.vector.tensor_copy(k2_hm[0:HALF, i], k2_hl[0:HALF, i]).then_inc(p_lo, 1)
                    if s in (NORMED_SLOT, NORMED_SLOT + 1) and not first:
                        normed(it - 1, (0, 1) if s == NORMED_SLOT else (2, 3))
                    if s == NORMED_SLOT + 3 and not first:
                        finish(it - 1)
                    if s in (3, 4) and not last:
                        ln1(it + 1, (0, 1) if s == 3 else (2, 3))
                    if s in (6, 7) and not last:
                        ln1_apply(it + 1, (0, 1) if s == 6 else (2, 3))

            quads(nc.vector, quad)
            normed(NQUAD - 1, range(T))
            finish(NQUAD - 1)

        @block.tensor
        def _(pe):
            MM, TR = nc.tensor.matmul, nc.tensor.transpose

            def product(dst, a, b, first=True, last=True):
                n = 0
                for (ah, al), (bh, bl) in zip(a, b):
                    for x, w in ((ah, bh), (ah, bl), (al, bh)):
                        ins = MM(dst, x, w, start=first and n == 0, stop=last and n == 3 * len(a) - 1,
                                 skip_group_check=True)
                        n += 1
                return ins

            pe.wait_ge(consts, 9)
            pe.wait_ge(cstep, 4)
            pe.wait_ge(w_in, 16 * 13)
            for c in range(DC):
                for a in range(DC):
                    ins = TR(bank[c][:, a * P:(a + 1) * P], st_wo2[:, a, c * P:(c + 1) * P], ident[:])
            ins.then_inc(w_ps, 1)
            pe.wait_ge(w_split, 8 + DC)
            for a in range(DC):
                for c in range(DC):
                    ins = MM(bank[2 + a][:, 0:D], wo2T[:, c, a * P:(a + 1) * P], st_wff[:, c], start=c == 0,
                             stop=c == DC - 1)
                ins.then_inc(w_ps, 1)
            for c in range(HC):
                ins = MM(bank[4][0:1, 0:D], bv_col[:, c:c + 1], st_wo[:, c], start=c == 0, stop=c == HC - 1)
            ins.then_inc(w_ps, 1)
            pe.wait_ge(w_split, 18)
            MM(bank[5][:, 0:D], ones_row[:], c_row[:], start=True, stop=True).then_inc(w_ps, 1)
            pe.wait_ge(w_bias, 5)
            pe.wait_ge(zeroed, 3)
            pe.wait_ge(picked, 4 * DC)

            def cols(x, c, t):
                return x[:, c, t * P:(t + 1) * P]

            def transposed(b, src):
                for c in range(DC):
                    ins = TR(b[:, c * P:(c + 1) * P], src[:, c * P:(c + 1) * P], ident[:])
                return ins

            def projected(b, j):
                if j < 2 * HC:
                    w, c = (1, j) if j < HC else (0, j - HC)
                    m = [(w1_hi[:, w, i, c * P:(c + 1) * P], w1_lo[:, w, i, c * P:(c + 1) * P]) for i in range(DC)]
                    n = [(xT_hi[:, i], xT_lo[:, i]) for i in range(DC)]
                else:
                    t, e = (j - 2 * HC) // 2, j % 2
                    m = [(cols(xT_hi, i, t), cols(xT_lo, i, t)) for i in range(DC)]
                    n = [(w1_hi[:, 2, i, e * 512:(e + 1) * 512], w1_lo[:, 2, i, e * 512:(e + 1) * 512])
                         for i in range(DC)]
                product(b[:], m, n).then_inc(p_ps, 1)

            for t in range(T):
                pe.wait_ge(xn_ok, t + 1)
                ge(pe, p_lo, t - 1)
                transposed(PB[(t + 1) % 2], xn[:, t]).then_inc(p_ps, 1)
            pe.wait_ge(p_lo, T)
            for j in range(PR - LATE):
                ge(pe, p_lo, T + j - 1)
                projected(PB[(j + 1) % 2], j)

            def project(it, last, n, w, i):
                m = p_before(last, n)
                if m is not None:
                    pe.wait_ge(p_lo, p_count(it, m))
                elif p_bank(last, n) == 1:
                    pe.wait_ge(m_neg, it * (2 * U) + U)
                else:
                    pe.wait_ge(p_lo, it * NPJ + PRO)
                b = PB[p_bank(last, n)]
                if w in ("p1", "late"):
                    if w == "p1" and i == 0:
                        pe.wait_ge(p_lo, p_job_of(it, last, "xn", T - 1))
                    projected(b, i)
                    return
                if w in ("xn", "x2"):
                    if w == "xn":
                        pe.wait_ge(xn_ok, it * T + (T + i + 1))
                    else:
                        pe.wait_ge(x2_ok, it * T + (i + 1))
                    transposed(b, xn[:, i] if w == "xn" else x2[:, i]).then_inc(p_ps, 1)
                    return
                if w == "qk2":
                    pe.wait_ge(p_lo, p_job_of(it, last, "x2", i))
                    for e in range(2):
                        for c in range(DC):
                            at = (e * DC + c) * P
                            ins = product(b[:, at:at + P],
                                          [(w2_hi[:, e, k, c * P:(c + 1) * P], w2_lo[:, e, k, c * P:(c + 1) * P])
                                           for k in range(DC)],
                                          [(x2T_hi[:, k], x2T_lo[:, k]) for k in range(DC)])
                    ins.then_inc(p_ps, 1)
                else:
                    product(b[:, 0:D], [(x2T_hi[:, k], x2T_lo[:, k]) for k in range(DC)],
                            [(w2_hi[:, 2, k], w2_lo[:, 2, k]) for k in range(DC)]).then_inc(p_ps, 1)

            def quad(it, first, last):
                for s in range(LAST):
                    u = s - 1
                    if 0 <= u < U:
                        pe.wait_ge(m_neg, it * (2 * U) + (u + 1))
                        ge(pe, m_sb, it * (2 * U) + u)
                        TR(MT[0:G, 0:P], neg_max[:, u % 2], ident_b[:]).then_inc(m_ps, 1)
                    v = s - V0 - 1
                    if 0 <= v < U:
                        pe.wait_ge(m_neg, it * (2 * U) + (U + v + 1))
                        pe.wait_ge(m_sb, it * (2 * U) + (U + v))
                        TR(MT[0:G, 0:P], neg_max[:, v % 2], ident_b[:]).then_inc(m_ps, 1)
                    if s < U:
                        t, g = s // NG, s % NG
                        if s >= 1:
                            pe.wait_ge(m_neg, it * (2 * U) + s)
                        else:
                            pe.wait_ge(p_lo, it * NPJ + PRO - 1)
                        MM(SM[:], ident_b[:], band[:].rearrange("p g n -> p (g n)"), start=True, stop=False,
                           skip_group_check=True)
                        for j in range(G):
                            c = g * 2 + j // 2
                            ins = MM(SM[:, j * P:(j + 1) * P], qz_hi[:, c, t, j % 2], cols(k_hi, c, t),
                                     start=False, stop=j == G - 1, skip_group_check=True)
                        ins.then_inc(sm_ps, 1)
                    v = s - V0
                    if 0 <= v < U:
                        t, g = v // NG, v % NG
                        c, h = g // 2, (g % 2) * G
                        if v < 2:
                            pe.wait_ge(e_exp, it * U + (U + v - 1))
                        else:
                            pe.wait_ge(f_exp, it * U + (v - 1))
                        if g < 2:
                            pe.wait_ge(q2z_in[t % 2][g], q2z_count(it, t))
                        MM(ST[v % 2][:], k2_hl[:, t, c, g % 2],
                           q2z[:, t % 2, 0, c, h:h + G].rearrange("p h n -> p (h n)"), start=True, stop=False,
                           skip_group_check=True).then_inc(s2_ps, 1)
                    for n, w, i in t_jobs(s, "o"):
                        pe.wait_ge(o_ok, it * U + (i + 1))
                        ge(pe, t_lo, t_count(it, n - 1))
                        transposed(TB, o_f[:, i % 2]).then_inc(t_ps, 1)
                    u = s - 1
                    if 0 <= u < U:
                        t, g = u // NG, u % NG
                        if u < 2:
                            ge(pe, f_exp, it * U)
                        else:
                            pe.wait_ge(e_exp, it * U + (u - 1))
                        for i in range(2):
                            c = g * 2 + i
                            product(ST[u % 2][:, i * 2 * P:(i + 1) * 2 * P],
                                    [(cols(k_hi, c, t), cols(k_lo, c, t))],
                                    [(qz_hi[:, c, t].rearrange("p h n -> p (h n)"),
                                      qz_lo[:, c, t].rearrange("p h n -> p (h n)"))], first=i == 0, last=False)
                        pe.wait_ge(m_sb, it * (2 * U) + (u + 1))
                        for j in range(G):
                            ins = MM(ST[u % 2][:, j * P:(j + 1) * P], pick[:, j], maxT[:, u % 2],
                                     start=False, stop=j == G - 1, skip_group_check=True)
                        ins.then_inc(st_ps, 1)
                    at_once = 1 if s >= V0 else 0
                    for n, w, i in p_jobs(s, last)[:at_once]:
                        project(it, last, n, w, i)
                    v = s - V0 - 1
                    if 0 <= v < U:
                        t, g = v // NG, v % NG
                        c, h = g // 2, (g % 2) * G
                        pe.wait_ge(m_sb, it * (2 * U) + (U + v + 1))
                        MM(ST[v % 2][:], k2_hm[:, t, c, g % 2],
                           q2z[0:HALF + G, t % 2, 1, c, h:h + G].rearrange("p h n -> p (h n)"), start=False,
                           stop=True, skip_group_check=True).then_inc(s2m_ps, 1)
                    for n, w, i in t_jobs(s, "z"):
                        pe.wait_ge(z_sb, it * T + (i + 1))
                        ge(pe, t_lo, t_count(it, n - 1))
                        transposed(TB, z_f[:]).then_inc(t_ps, 1)
                    u = s - 4
                    if 0 <= u < U:
                        t, g = u // NG, u % NG
                        pe.wait_ge(e_l, it * U + (u + 1))
                        if u >= 1:
                            pe.wait_ge(o_ok, it * U + u)
                        else:
                            ge(pe, z_sb, it * T)
                        for j in range(G):
                            h = g * G + j
                            ins = product(PV[:, j * VW:(j + 1) * VW],
                                          [(e_hi[:, u % 3, j * P:(j + 1) * P], e_lo[:, u % 3, j * P:(j + 1) * P])],
                                          [(v_hi[:, t, h], v_lo[:, t, h])])
                        ins.then_inc(pv_ps, 1)
                    u = s - 6
                    if 0 <= u < U:
                        t, g = u // NG, u % NG
                        pe.wait_ge(t_lo, t_job_of(it, "o", u))
                        if g == 0 and t == 0:
                            ge(pe, z2_ok, it * (3 * T))
                        elif g == 0:
                            pe.wait_ge(h2_ok, it * T + t)
                        ins = product(WO[:, 0:D],
                                      [(oT_hi[:, u % 2, c * P:(c + 1) * P], oT_lo[:, u % 2, c * P:(c + 1) * P])
                                       for c in range(2)],
                                      [(wo_hi[:, g * 2 + c], wo_lo[:, g * 2 + c]) for c in range(2)],
                                      first=g == 0, last=g == NG - 1)
                        if g == NG - 1:
                            ins.then_inc(wo_ps, 1)
                    if s in Z_SLOT:
                        t = Z_SLOT[s]
                        pe.wait_ge(v2n_l, it * T + (t + 1))
                        pe.wait_ge(f_l, it * U + (t + 1) * NG)
                        if t >= 1:
                            pe.wait_ge(z_sb, it * T + t)
                        else:
                            pe.wait_ge(o_ok, it * U + U)
                        for h in range(H):
                            g, j = h // G, h % G
                            w = slice(h * DH2, (h + 1) * DH2)
                            ins = product(PV[:, w], [(f_hi[:, t % 2, g, j * P:(j + 1) * P],
                                                      f_lo[:, t % 2, g, j * P:(j + 1) * P])],
                                          [(v2n_hi[:, w], v2n_lo[:, w])])
                        ins.then_inc(z_ps, 1)
                    if s in WF_SLOT:
                        t = WF_SLOT[s]
                        pe.wait_ge(t_lo, t_job_of(it, "z", t))
                        if t >= 1:
                            pe.wait_ge(z2_ok, it * (3 * T) + 3 * t)
                        else:
                            pe.wait_ge(h2_ok, it * T + T)
                        product(WO[:], [(zT_hi[:, c * P:(c + 1) * P], zT_lo[:, c * P:(c + 1) * P])
                                        for c in range(DC)],
                                [(wf_hi[:, c], wf_lo[:, c]) for c in range(DC)]).then_inc(wf_ps, 1)
                    for n, w, i in p_jobs(s, last)[at_once:]:
                        project(it, last, n, w, i)

            quads(nc.tensor, quad)


_INS = ['L0_tok_weight', 'L0_attn_Wq', 'L0_attn_bq', 'L0_attn_Wk', 'L0_attn_bk', 'L0_attn_Wv', 'L0_attn_bv',
        'L0_attn_Wo', 'L0_attn_bo', 'L0_ffn_Wq', 'L0_ffn_Wk', 'L0_ffn_Wv', 'L0_ffn_Wo', 'L0_ffn_Wff']


def kernel(**inputs):
    import numpy as _np
    import concourse.bacc as _bacc
    from concourse import mybir as _mybir
    from concourse.bass_utils import run_bass_kernel_spmd as _run

    nc = _bacc.Bacc("TRN2", target_bir_lowering=False, num_devices=1)
    x = _np.asarray(inputs["x"])
    tok = _np.ascontiguousarray(x.T)
    arrays = {"in_x_dram": tok}
    args = [nc.dram_tensor("in_x_dram", tok.shape, _mybir.dt.from_np(tok.dtype), kind="ExternalInput").ap()]
    for name in _INS:
        a = _np.ascontiguousarray(inputs[name])
        arrays[f"in_{name}_dram"] = a
        args.append(nc.dram_tensor(f"in_{name}_dram", a.shape, _mybir.dt.from_np(a.dtype), kind="ExternalInput").ap())
    shape = (x.shape[0], x.shape[1], inputs["L0_tok_weight"].shape[1])
    args.append(nc.dram_tensor("out_0_dram", shape, _mybir.dt.float32, kind="ExternalOutput").ap())
    tower_kernel(nc, *args)
    nc.compile()
    r = _run(nc, [arrays], core_ids=[0])
    return r.results[0]["out_0_dram"]
```
